# Optimizing a Trainium2 kernel written in Bass

```python
import numpy as np
import jax
import jax.numpy as jnp

def _softmax(x, axis=-1):
    return jax.nn.softmax(x, axis=axis)

def _gelu(x):
    return jax.nn.gelu(x, approximate=True)

def _silu(x):
    return jax.nn.silu(x)

def _sigmoid(x):
    return jax.nn.sigmoid(x)

def _layernorm(x, axis=-1, eps=1e-05):
    m = jnp.mean(x, axis=axis, keepdims=True)
    v = jnp.var(x, axis=axis, keepdims=True)
    return (x - m) / jnp.sqrt(v + eps)

def _scatter_add(tgt, idx, src, axis=0):
    return tgt.at[idx].add(src)

def _segment_sum(src, seg, n):
    return jax.ops.segment_sum(src, seg, n)
kernel_name = 'mk_gnn_preln_d2_gnn_r8_3218f6'

def setup_inputs(seed: int=0):
    np.random.seed(seed)
    _w = jnp.asarray

    def _rec_inputs():
        import jax
        import jax.numpy as jnp
        _gk = jax.random.key(seed)
        x = -6.415e-05 + 1 * jax.random.normal(jax.random.fold_in(_gk, 1), (2500, 512), jnp.float32)
        src = jax.random.randint(jax.random.fold_in(_gk, 2), (40000,), 0, 2500, jnp.int32)
        dst = jax.random.randint(jax.random.fold_in(_gk, 3), (40000,), 0, 2500, jnp.int32)
        _o = jnp.argsort(dst, stable=True)
        src = src[_o]
        dst = dst[_o]
        return (x, src, dst)
    x, src, dst = _rec_inputs()

    def _L0_gnn_setup():
        import jax, jax.numpy as jnp
        import numpy as np
        N_NODES = 2500
        N_EDGES = 40000
        D_IN = 512
        D_OUT = 512
        key = jax.random.key(seed)
        k1, k2, k3, k4, k5, k6 = jax.random.split(key, 6)
        stdv = 1.0 / np.sqrt(D_OUT)
        return {'h': jax.random.normal(k1, (N_NODES, D_IN), dtype=jnp.float32), 'weight': jax.random.uniform(k2, (D_IN, D_OUT), dtype=jnp.float32, minval=-stdv, maxval=stdv), 'bias': jax.random.uniform(k3, (D_OUT,), dtype=jnp.float32, minval=-stdv, maxval=stdv), 'norm': jax.random.uniform(k4, (N_NODES, 1), dtype=jnp.float32, minval=0.05, maxval=1.0), 'src': jax.random.randint(k5, (N_EDGES,), 0, N_NODES, dtype=jnp.int32), 'dst': jax.random.randint(k6, (N_EDGES,), 0, N_NODES, dtype=jnp.int32)}
    _L0_gnn_all = _L0_gnn_setup()
    _L0_gnn_in = {k: v for k, v in _L0_gnn_all.items() if k in ('weight', 'bias')}
    del _L0_gnn_all

    def _L1_gnn_setup():
        import jax, jax.numpy as jnp
        import numpy as np
        D = 512
        H = 8
        DH = D // H
        F = 256
        L = 2
        N = 2500
        E = 40000
        EPS = 1e-05

        def _xavier(key, shape):
            fan_out, fan_in = (shape[-2], shape[-1])
            lim = float(np.sqrt(6.0 / (fan_in + fan_out)))
            return jax.random.uniform(key, shape, jnp.float32, -lim, lim)

        def _batchnorm(x, g, b):
            mu = jnp.mean(x, axis=0)
            var = jnp.mean(jnp.square(x - mu), axis=0)
            return (x - mu) * jax.lax.rsqrt(var + EPS) * g + b

        def _layernorm(x, g, b):
            mu = jnp.mean(x, axis=-1, keepdims=True)
            var = jnp.mean(jnp.square(x - mu), axis=-1, keepdims=True)
            return (x - mu) * jax.lax.rsqrt(var + EPS) * g + b
        key = jax.random.key(seed)
        ks = jax.random.split(key, 12)
        src = jax.random.normal(ks[0], (N, D), jnp.float32)
        edge_index = jax.random.randint(ks[1], (2, E), 0, N)
        return {'src': src, 'edge_index': edge_index, 'Wq': _xavier(ks[2], (L, D, D)), 'bq': jnp.zeros((L, D), jnp.float32), 'Wk': _xavier(ks[3], (L, D, D)), 'Wv': _xavier(ks[4], (L, D, D)), 'Wo': _xavier(ks[5], (L, D, D)), 'bo': jnp.zeros((L, D), jnp.float32), 'W1': _xavier(ks[6], (L, F, D)), 'b1': jnp.zeros((L, F), jnp.float32), 'W2': _xavier(ks[7], (L, D, F)), 'b2': jnp.zeros((L, D), jnp.float32), 'g1': jnp.ones((L, D), jnp.float32), 'beta1': jnp.zeros((L, D), jnp.float32), 'g2': jnp.ones((L, D), jnp.float32), 'beta2': jnp.zeros((L, D), jnp.float32), 'ln_g': jnp.ones((D,), jnp.float32), 'ln_b': jnp.zeros((D,), jnp.float32)}
    _L1_gnn_all = _L1_gnn_setup()
    _L1_gnn_in = {k: v for k, v in _L1_gnn_all.items() if k in ('Wq', 'bq', 'Wk', 'Wv', 'Wo', 'bo', 'W1', 'b1', 'W2', 'b2', 'g1', 'beta1', 'g2', 'beta2', 'ln_g', 'ln_b')}
    del _L1_gnn_all
    return {'x': x, 'src': src, 'dst': dst, 'L0_gnn_weight': _L0_gnn_in['weight'], 'L0_gnn_bias': _L0_gnn_in['bias'], 'L1_gnn_Wq': _L1_gnn_in['Wq'], 'L1_gnn_bq': _L1_gnn_in['bq'], 'L1_gnn_Wk': _L1_gnn_in['Wk'], 'L1_gnn_Wv': _L1_gnn_in['Wv'], 'L1_gnn_Wo': _L1_gnn_in['Wo'], 'L1_gnn_bo': _L1_gnn_in['bo'], 'L1_gnn_W1': _L1_gnn_in['W1'], 'L1_gnn_b1': _L1_gnn_in['b1'], 'L1_gnn_W2': _L1_gnn_in['W2'], 'L1_gnn_b2': _L1_gnn_in['b2'], 'L1_gnn_g1': _L1_gnn_in['g1'], 'L1_gnn_beta1': _L1_gnn_in['beta1'], 'L1_gnn_g2': _L1_gnn_in['g2'], 'L1_gnn_beta2': _L1_gnn_in['beta2'], 'L1_gnn_ln_g': _L1_gnn_in['ln_g'], 'L1_gnn_ln_b': _L1_gnn_in['ln_b']}

def reference(x, src, dst, L0_gnn_weight, L0_gnn_bias, L1_gnn_Wq, L1_gnn_bq, L1_gnn_Wk, L1_gnn_Wv, L1_gnn_Wo, L1_gnn_bo, L1_gnn_W1, L1_gnn_b1, L1_gnn_W2, L1_gnn_b2, L1_gnn_g1, L1_gnn_beta1, L1_gnn_g2, L1_gnn_beta2, L1_gnn_ln_g, L1_gnn_ln_b):
    import jax
    import jax.numpy as jnp

    def _L0_gnn_ref(h, weight, bias, norm, src, dst):
        import jax, jax.numpy as jnp
        import numpy as np
        N_NODES = 2500
        N_EDGES = 40000
        D_IN = 512
        D_OUT = 512
        hw = norm * jnp.matmul(h, weight)
        msg = hw[src]
        agg = jax.ops.segment_sum(msg, dst, num_segments=N_NODES)
        out = agg * norm + bias
        return jax.nn.relu(out)

    def _L1_gnn_ref(src, edge_index, Wq, bq, Wk, Wv, Wo, bo, W1, b1, W2, b2, g1, beta1, g2, beta2, ln_g, ln_b):
        import jax, jax.numpy as jnp
        import numpy as np
        D = 512
        H = 8
        DH = D // H
        F = 256
        L = 2
        N = 2500
        E = 40000
        EPS = 1e-05

        def _xavier(key, shape):
            fan_out, fan_in = (shape[-2], shape[-1])
            lim = float(np.sqrt(6.0 / (fan_in + fan_out)))
            return jax.random.uniform(key, shape, jnp.float32, -lim, lim)

        def _batchnorm(x, g, b):
            mu = jnp.mean(x, axis=0)
            var = jnp.mean(jnp.square(x - mu), axis=0)
            return (x - mu) * jax.lax.rsqrt(var + EPS) * g + b

        def _layernorm(x, g, b):
            mu = jnp.mean(x, axis=-1, keepdims=True)
            var = jnp.mean(jnp.square(x - mu), axis=-1, keepdims=True)
            return (x - mu) * jax.lax.rsqrt(var + EPS) * g + b
        n = src.shape[0]
        scaling = float(DH) ** (-0.5)
        tgt = edge_index[1]
        srcidx = edge_index[0]
        x = src
        for l in range(L):
            q = ((x @ Wq[l].T + bq[l]) * scaling).reshape(n, H, DH)
            k = (x @ Wk[l].T).reshape(n, H, DH)
            v = (x @ Wv[l].T).reshape(n, H, DH)
            scores = jnp.einsum('ehd,ehd->eh', q[tgt], k[srcidx])
            m = jax.ops.segment_max(scores, tgt, num_segments=n)
            p = jnp.exp(scores - m[tgt])
            s = jax.ops.segment_sum(p, tgt, num_segments=n)
            w = p / (s[tgt] + 1e-16)
            agg = jax.ops.segment_sum(w[:, :, None] * v[srcidx], tgt, num_segments=n)
            attn = agg.reshape(n, D) @ Wo[l].T + bo[l]
            x = _batchnorm(x + attn, g1[l], beta1[l])
            ff = jax.nn.relu(x @ W1[l].T + b1[l]) @ W2[l].T + b2[l]
            x = _batchnorm(x + ff, g2[l], beta2[l])
        return _layernorm(x, ln_g, ln_b)
    edge_index = jnp.stack([src, dst])
    deg = jnp.maximum(jax.ops.segment_sum(jnp.ones(dst.shape, jnp.float32), dst, num_segments=2500), 1.0)
    deg_isqrt = deg ** (-0.5)
    h = jnp.maximum(_layernorm(x, axis=-1), 0.0)
    x = x + _L0_gnn_ref(h, L0_gnn_weight, L0_gnn_bias, deg_isqrt[:, None], src, dst)
    h = jnp.maximum(_layernorm(x, axis=-1), 0.0)
    x = x + _L1_gnn_ref(h, edge_index, L1_gnn_Wq, L1_gnn_bq, L1_gnn_Wk, L1_gnn_Wv, L1_gnn_Wo, L1_gnn_bo, L1_gnn_W1, L1_gnn_b1, L1_gnn_W2, L1_gnn_b2, L1_gnn_g1, L1_gnn_beta1, L1_gnn_g2, L1_gnn_beta2, L1_gnn_ln_g, L1_gnn_ln_b)
    return x

_drawn_inputs = setup_inputs


def setup_inputs(seed=0):
    import zlib

    import numpy as np

    out = dict(_drawn_inputs(seed))
    spreads = {'L1_gnn_bq': (0.0, 0.361),
     'L1_gnn_bo': (0.0, 0.8),
     'L1_gnn_b1': (0.0, 0.1),
     'L1_gnn_b2': (0.0, 0.8),
     'L1_gnn_g1': (1.0, 0.2),
     'L1_gnn_beta1': (0.0, 0.1),
     'L1_gnn_g2': (1.0, 0.2),
     'L1_gnn_beta2': (0.0, 0.1),
     'L1_gnn_ln_g': (1.0, 0.2),
     'L1_gnn_ln_b': (0.0, 0.1)}
    factors = {'L0_gnn_bias': 3.869}
    for name, (base, spread) in spreads.items():
        noise = np.random.default_rng([zlib.crc32(name.encode()), seed]).standard_normal(out[name].shape)
        drawn = base * np.exp(spread * noise) if base else spread * noise
        out[name] = jnp.asarray(drawn.astype(out[name].dtype))
    for name, factor in factors.items():
        out[name] = (out[name] * factor).astype(out[name].dtype)
    return out
```

```python
from contextlib import ExitStack

import concourse.bass as bass
from concourse import mybir

F32 = mybir.dt.float32
F16 = mybir.dt.float16
BF16 = mybir.dt.bfloat16
I32 = mybir.dt.int32
U32 = mybir.dt.uint32
ALU = mybir.AluOpType
ACT = mybir.ActivationFunctionType
AXX = mybir.AxisListType.X

N = 2500
E = 40000
D = 512
H = 8
DH = D // H
FF = 256
L = 2
EPS = 1e-5
SCALING = float(DH) ** -0.5

P = 125
NT = N // P
FC = D // 128
HC = FF // 128
BANK = 512

EP = 125
NCOL = E // EP
GC = 8
NG = NCOL // GC
GE = GC * EP
LATER = 4096.0

ZCOLS = 6112
ZDMAS = 8
ZERO_FIRST = 16
TABLE = 128 * ZCOLS * ZDMAS
assert TABLE >= N * N + GE

MASKED = -1.0e30
FLOOR = -1.0e20

CH = 250
NCH = N // CH
KC = 500
SB = 2
TB = 4
HEAD0 = 3
NKC = N // KC
BPC = KC // P
UNITS = 2 * H
USES = H * NKC + 2


def apart(engine, waits_met):
    engine.sem_inc(waits_met, 1)


class Steps:

    def __init__(self, engine, semaphore, base=0):
        self.engine, self.semaphore, self.base, self.n = engine, semaphore, base, 0

    def done(self, instruction):
        instruction.then_inc(self.semaphore, 1)
        self.n += 1

    def wait(self, but=0):
        self.engine.wait_ge(self.semaphore, self.base + self.n - but)


def gnn_kernel(nc, x, src_cols, dst_cols, src_row, dst_row, w0, bias0, wq, wk, wv, wo, w1, w2,
               vectors, lng, lnb, out):
    top = ExitStack()

    def sem(name):
        return top.enter_context(nc.semaphore(name))

    def dram(name, shape, dt):
        return nc.dram_tensor(name, shape, dt, kind="Internal").ap()

    def psum(ctx, name, shape, dt=F32):
        return ctx.enter_context(nc.psum_tensor(name, shape, dt))

    def sb(ctx, name, shape, dt=F32):
        return ctx.enter_context(nc.sbuf_tensor(name, shape, dt))

    counts = dram("counts", [TABLE, 1], F32)
    counts_rows = counts[0:N * N, :].rearrange("(n m) o -> n (m o)", m=N)
    counts_flat = counts.rearrange("(p a) o -> p (a o)", p=128)
    bias_rows = dram("bias_rows", [N, N], F32)
    deg_flat = dram("deg_flat", [2560, 1], F32)
    x1_rows = dram("x1_rows", [N, D], F32)
    scrap_row = dram("scrap_row", [1, NT], F32)
    q_feat = dram("q_feat", [2 * D, N], F16)

    with top:
        identity = sb(top, "identity", [128, 128])
        eps_col = sb(top, "eps_col", [128, 1])
        consts_ready = sem("consts_ready")
        dve_steps = sem("dve_steps")
        waits_met = sem("waits_met")

        with ExitStack() as early:
            x_sb = sb(early, "x_sb", [P, NT, D])
            hw = sb(early, "hw", [P, NT, D])
            norm = sb(early, "norm", [P, NT])
            edges_and_degrees(nc, sem, psum, sb, locals())
            aggregate(nc, sem, psum, sb, locals())
        with ExitStack() as late:
            xt = sb(late, "xt", [128, FC, N])
            second_norm(nc, sem, psum, sb, locals())
            transformer(nc, sem, psum, sb, locals())
            final_norm(nc, sem, psum, sb, locals())


def edges_and_degrees(nc, sem, psum, sb, g):
    x, w0 = g["x"], g["w0"]
    src_cols, dst_cols, src_row, dst_row = g["src_cols"], g["dst_cols"], g["src_row"], g["dst_row"]
    counts, counts_flat, deg_flat = g["counts"], g["counts_flat"], g["deg_flat"]
    x_sb, hw, norm = g["x_sb"], g["hw"], g["norm"]
    identity, eps_col, consts_ready = g["identity"], g["eps_col"], g["consts_ready"]
    HI, LO = 40, 64
    QC = NCOL // 4

    with ExitStack() as ctx:
        w0_sb = sb(ctx, "w0_sb", [128, FC, D])
        zeros = sb(ctx, "zeros", [128, ZCOLS])
        earlier = sb(ctx, "earlier", [EP, 2 * GE - EP])
        src_i = sb(ctx, "src_i", [EP, NCOL], I32)
        dst_i = sb(ctx, "dst_i", [EP, NCOL], I32)
        digit_i = sb(ctx, "digit_i", [EP, 2, NCOL], I32)
        digit = sb(ctx, "digit", [EP, 2, NCOL], BF16)
        ramp_i = sb(ctx, "ramp_i", [EP, LO], I32)
        ramp = sb(ctx, "ramp", [EP, LO], BF16)
        onehot_hi = [sb(ctx, f"onehot_hi{b}", [EP, QC, HI], BF16) for b in range(2)]
        onehot_lo = [sb(ctx, f"onehot_lo{b}", [EP, QC, LO], BF16) for b in range(2)]
        pair = sb(ctx, "pair", [EP, NCOL])
        spare_i = sb(ctx, "spare_i", [EP, NCOL], I32)
        to_spare = sb(ctx, "to_spare", [EP, NCOL])
        srow = [sb(ctx, f"srow{b}", [EP, GE], I32) for b in range(2)]
        drow = [sb(ctx, f"drow{b}", [EP, GE], I32) for b in range(2)]
        pair_row = sb(ctx, "pair_row", [EP, GE])
        matches = [sb(ctx, f"matches{r}", [EP, GE], BF16) for r in range(2)]
        pair_cols = [sb(ctx, f"pair_cols{b}", [EP, 2 * GC]) for b in range(2)]
        tally = [sb(ctx, f"tally{b}", [EP, GC]) for b in range(2)]
        moved = sb(ctx, "moved", [EP, GC])
        cell = [sb(ctx, f"cell{b}", [EP, GC], U32) for b in range(2)]
        deg_sb = sb(ctx, "deg_sb", [HI, LO])
        deg_col = sb(ctx, "deg_col", [P, NT])
        deg_root = sb(ctx, "deg_root", [P, NT])
        stats = sb(ctx, "stats", [P, NT, 6])
        mv = sb(ctx, "mv", [P, NT, 2])
        root = sb(ctx, "root", [P, NT])
        rstd = sb(ctx, "rstd", [P, NT])
        shift = sb(ctx, "shift", [P, NT])
        h = [sb(ctx, f"h{b}", [P, D]) for b in range(2)]
        ht = [sb(ctx, f"ht{b}", [128, FC, P]) for b in range(2)]
        deg_ps = psum(ctx, "deg_ps", [HI, LO])
        ht_ps = [psum(ctx, f"ht_ps{b}", [128, BANK]) for b in range(2)]
        hw_ps = [psum(ctx, f"hw_ps{b}", [128, BANK]) for b in range(2)]

        edges_loaded = sem("edges_loaded")
        x_loaded = sem("x_loaded")
        w0_loaded = sem("w0_loaded")
        zeros_ready = sem("zeros_ready")
        ramps_ready = sem("ramps_ready")
        rows_loaded = [sem("rows_loaded0"), sem("rows_loaded1")]
        rows_used = sem("rows_used")
        table_writes = sem("table_writes")
        cells_ready = sem("cells_ready")
        onehots_ready = sem("onehots_ready")
        onehots_used = sem("onehots_used")
        deg_ready = sem("deg_ready")
        deg_stored = sem("deg_stored")
        deg_loaded = sem("deg_loaded")
        variances_ready = sem("variances_ready")
        roots_ready = sem("roots_ready")
        scales_ready = sem("scales_ready")
        norm_ready = sem("norm_ready")
        h_ready = sem("h_ready")
        h_turned = sem("h_turned")
        ht_ready = sem("ht_ready")
        hw_summed = sem("hw_summed")
        hw_ready = sem("hw_ready")
        dve_steps, waits_met = g["dve_steps"], g["waits_met"]

        with nc.Block() as block:
            @block.sync
            def _(sp):
                sp.dma_start(dst_i[:, :], dst_cols).then_inc(edges_loaded, 16)
                sp.dma_start(src_i[:, :], src_cols).then_inc(edges_loaded, 16)
                with sp.Fori(0, NG // 2) as i:
                    for b in range(2):
                        sp.wait_ge(rows_used, 2 * i + b + 1)
                        at = bass.ts(2 * i + b, GE)
                        sp.dma_start(drow[b][:, :], dst_row[:, at].broadcast_to([EP, GE])).then_inc(rows_loaded[b], 16)
                        sp.dma_start(srow[b][:, :], src_row[:, at].broadcast_to([EP, GE])).then_inc(rows_loaded[b], 16)
                sp.wait_ge(table_writes, ZERO_FIRST + 16 * GC * (NG + 1))

            @block.gpsimd
            def _(pool):
                pool.memset(identity[:, :], 0.0).then_inc(consts_ready, 1)
                pool.memset(eps_col[:, :], EPS).then_inc(consts_ready, 1)
                pool.wait_ge(consts_ready, 2)
                pool.affine_select(out=identity[:, :], in_=identity[:, :], compare_op=ALU.not_equal, fill=1.0,
                                   base=0, pattern=[[-1, 128]], channel_multiplier=1).then_inc(consts_ready, 1)
                pool.iota(ramp_i[:, :], pattern=[[1, LO]], base=0, channel_multiplier=0).then_inc(ramps_ready, 1)
                pool.iota(spare_i[:, :], pattern=[[0, NG], [EP, GC]], base=0,
                          channel_multiplier=1).then_inc(ramps_ready, 1)
                pool.memset(earlier[:, :], 1.0 + LATER).then_inc(ramps_ready, 1)
                pool.wait_ge(ramps_ready, 3)
                pool.affine_select(out=earlier[:, :], in_=earlier[:, :], compare_op=ALU.is_gt, fill=1.0,
                                   base=GE - EP, pattern=[[-1, 2 * GE - EP]], channel_multiplier=1
                                   ).then_inc(ramps_ready, 1)
                pool.wait_ge(zeros_ready, 1)
                pool.dma_start(counts_flat[0:16, 0:GC], zeros[0:16, 0:GC]).then_inc(table_writes, 16)
                for k in range(ZDMAS):
                    if k == 0:
                        pool.wait_ge(table_writes, ZERO_FIRST)
                    pool.dma_start(counts_flat[:, k * ZCOLS:(k + 1) * ZCOLS], zeros[:, :]).then_inc(table_writes, 16)
                with pool.Fori(0, NG // 2) as i:
                    for b in range(2):
                        pool.wait_ge(cells_ready, 2 * i + b + 1)
                        pool.wait_ge(table_writes, ZERO_FIRST + 16 * GC * (2 * i + b + 1))
                        apart(pool, waits_met)
                        for c in range(GC):
                            pool.indirect_dma_start(counts, bass.IndirectOffsetOnAxis(cell[b][:, c:c + 1], 0),
                                                    tally[b][:, c:c + 1], None,
                                                    compute_op=ALU.add).then_inc(table_writes, 16)

            @block.vector
            def _(dve):
                steps = Steps(dve, dve_steps)
                dve.sem_inc(rows_used, 2)
                dve.memset(zeros[:, :], 0.0).then_inc(zeros_ready, 1)
                dve.wait_ge(edges_loaded, 32)
                dve.wait_ge(ramps_ready, 4)
                steps.done(dve.tensor_scalar(digit_i[:, 0, :], dst_i[:, :], 6, None, ALU.logical_shift_right))
                steps.done(dve.tensor_scalar(digit_i[:, 1, :], dst_i[:, :], LO - 1, None, ALU.bitwise_and))
                steps.done(dve.tensor_copy(ramp[:, :], ramp_i[:, :]))
                steps.done(dve.scalar_tensor_tensor(pair[:, :], dst_i[:, :], float(N), src_i[:, :], ALU.mult, ALU.add))
                steps.wait()
                steps.done(dve.tensor_copy(digit[:, :, :], digit_i[:, :, :]))
                steps.done(dve.scalar_tensor_tensor(to_spare[:, :], spare_i[:, :], float(N * N), pair[:, :], ALU.add, ALU.subtract))
                steps.wait()
                for q in range(4):
                    if q >= 2:
                        dve.wait_ge(onehots_used, q - 1)
                    for d, (hot, width) in enumerate(((onehot_hi, HI), (onehot_lo, LO))):
                        dve.tensor_tensor(hot[q % 2][:, :, :],
                                          digit[:, d, q * QC:(q + 1) * QC].unsqueeze(2).broadcast_to([EP, QC, width]),
                                          ramp[:, 0:width].unsqueeze(1).broadcast_to([EP, QC, width]),
                                          ALU.is_equal).then_inc(onehots_ready, 1)
                dve.wait_ge(x_loaded, 16)
                for t in range(NT):
                    steps.done(dve.bn_stats(stats[:, t, :], x_sb[:, t, :]))
                steps.wait()
                for t in range(NT):
                    ins = dve.bn_aggr(mv[:, t, :], stats[:, t, :])
                ins.then_inc(variances_ready, 1)
                dve.wait_ge(roots_ready, 1)
                steps.done(dve.reciprocal(rstd[:, :], root[:, :]))
                steps.wait()
                dve.scalar_tensor_tensor(shift[:, :], mv[:, :, 0], -1.0, rstd[:, :], ALU.mult, ALU.mult).then_inc(scales_ready, 1)
                dve.wait_ge(onehots_used, 4)
                dve.tensor_scalar(deg_sb[:, :], deg_ps[:, :], 1.0, None, ALU.max).then_inc(deg_ready, 1)
                dve.wait_ge(roots_ready, 2)
                dve.reciprocal(norm[:, :], deg_root[:, :]).then_inc(norm_ready, 1)

                per_turn = 2 * (GC + 4)
                with dve.Fori(0, NG // 2) as i:
                    turn = Steps(dve, dve_steps, steps.n + per_turn * i)
                    for b in range(2):
                        dve.wait_ge(rows_loaded[b], 32 * (i + 1))
                        dve.wait_ge(table_writes, ZERO_FIRST + 16 * GC * (2 * i + b))
                        dve.scalar_tensor_tensor(pair_row[:, :], drow[b][:, :], float(N), srow[b][:, :],
                                                 ALU.mult, ALU.add).then_inc(rows_used, 1)
                        dve.wait_ge(rows_used, 2 * i + b + 3)
                        at = bass.ts(2 * i + b, GC)
                        turn.done(dve.tensor_copy(pair_cols[b][:, 0:GC], pair[:, at]))
                        turn.done(dve.tensor_copy(pair_cols[b][:, GC:2 * GC], to_spare[:, at]))
                        turn.wait()
                        for c in range(GC):
                            if c >= 2:
                                turn.wait(but=1)
                            turn.done(dve.scalar_tensor_tensor(
                                matches[c % 2][:, :], pair_row[:, :], pair_cols[b][:, c:c + 1],
                                earlier[:, GE - EP - c * EP:2 * GE - EP - c * EP],
                                ALU.is_equal, ALU.mult, accum_out=tally[b][:, c:c + 1]))
                        turn.wait()
                        turn.done(dve.scalar_tensor_tensor(moved[:, :], tally[b][:, :], LATER - 0.5,
                                                           pair_cols[b][:, GC:2 * GC], ALU.is_gt, ALU.mult))
                        turn.wait()
                        turn.done(dve.tensor_tensor(cell[b][:, :], moved[:, :], pair_cols[b][:, 0:GC], ALU.add))
                        turn.wait()
                        dve.sem_inc(cells_ready, 1)
                    assert turn.n == per_turn

            @block.scalar
            def _(act):
                act.dma_start(x_sb[:, :, :], x.rearrange("(t p) d -> p t d", p=P)).then_inc(x_loaded, 16)
                act.dma_start(w0_sb[:, :, :], w0.rearrange("(c p) d -> p c d", p=128)).then_inc(w0_loaded, 16)
                act.wait_ge(consts_ready, 3)
                act.wait_ge(variances_ready, 1)
                act.activation(root[:, :], mv[:, :, 1], ACT.Sqrt, bias=eps_col[0:P, :]).then_inc(roots_ready, 1)
                act.wait_ge(deg_ready, 1)
                act.dma_start(deg_flat.rearrange("(a b) o -> a (b o)", b=LO), deg_sb[:, :]).then_inc(deg_stored, 16)
                act.wait_ge(deg_stored, 16)
                act.dma_start(deg_col[:, :], deg_flat[0:N, :].rearrange("(t p) o -> p (t o)", p=P),
                              allow_slow_non_contiguous=True).then_inc(deg_loaded, 16)
                act.wait_ge(deg_loaded, 16)
                act.activation(deg_root[:, :], deg_col[:, :], ACT.Sqrt).then_inc(roots_ready, 1)
                act.wait_ge(scales_ready, 1)
                act.wait_ge(norm_ready, 1)
                with act.Fori(0, NT // 2) as i:
                    for b in range(2):
                        t = 2 * i + b
                        act.wait_ge(h_turned, t + 1)
                        act.activation(h[b][:, :], x_sb[:, bass.ds(t, 1), :].rearrange("p o d -> p (o d)"), ACT.Relu,
                                       bias=shift[:, bass.ds(t, 1)], scale=rstd[:, bass.ds(t, 1)]).then_inc(h_ready, 1)
                        act.wait_ge(h_turned, t + 2)
                        act.copy(ht[b][:, :, :], ht_ps[b][:, 0:FC * P].rearrange("p (c n) -> p c n", c=FC)).then_inc(ht_ready, 1)
                        act.wait_ge(hw_summed, t + 1)
                        act.activation(hw[:, bass.ds(t, 1), :].rearrange("p o d -> p (o d)"), hw_ps[b][0:P, :],
                                       ACT.Copy, scale=norm[:, bass.ds(t, 1)]).then_inc(hw_ready, 1)

            @block.tensor
            def _(pe):
                for q in range(4):
                    pe.wait_ge(onehots_ready, 2 * (q + 1))
                    for c in range(QC):
                        mm = pe.matmul(deg_ps[:, :], lhsT=onehot_hi[q % 2][:, c, :], rhs=onehot_lo[q % 2][:, c, :],
                                       start=(q == 0 and c == 0), stop=(q == 3 and c == QC - 1))
                    mm.then_inc(onehots_used, 1)
                pe.wait_ge(w0_loaded, 16)
                pe.wait_ge(consts_ready, 3)
                pe.sem_inc(h_turned, 1)
                with pe.Fori(0, NT // 2) as i:
                    for b in range(2):
                        t = 2 * i + b
                        pe.wait_ge(h_ready, t + 1)
                        for c in range(FC):
                            mm = pe.transpose(ht_ps[b][:, c * P:(c + 1) * P], h[b][:, c * 128:(c + 1) * 128], identity[0:P, 0:P])
                        mm.then_inc(h_turned, 1)
                        pe.wait_ge(ht_ready, t + 1)
                        for c in range(FC):
                            mm = pe.matmul(hw_ps[b][0:P, :], lhsT=ht[b][:, c, :], rhs=w0_sb[:, c, :],
                                           start=(c == 0), stop=(c == FC - 1))
                        mm.then_inc(hw_summed, 1)


def aggregate(nc, sem, psum, sb, g):
    counts_rows, bias_rows, x1_rows, bias0 = g["counts_rows"], g["bias_rows"], g["x1_rows"], g["bias0"]
    x_sb, hw, norm, identity, scrap_row = g["x_sb"], g["hw"], g["norm"], g["identity"], g["scrap_row"]
    with ExitStack() as ctx:
        cnt = [sb(ctx, f"cnt{b}", [P, N]) for b in range(2)]
        least1 = sb(ctx, "least1", [P, N])
        logc = sb(ctx, "logc", [P, N])
        bias = [sb(ctx, f"edge_bias{b}", [P, N]) for b in range(2)]
        cnt_t = [sb(ctx, f"cnt_t{r}", [P, KC]) for r in range(2)]
        bias0_sb = sb(ctx, "bias0_sb", [P, D])
        conv = sb(ctx, "conv", [P, D])
        turn_ps = [psum(ctx, f"turn_ps{r}", [P, BANK]) for r in range(2)]
        agg_ps = [psum(ctx, f"agg_ps{b}", [P, BANK]) for b in range(2)]

        cnt_loaded = [sem("cnt_loaded0"), sem("cnt_loaded1")]
        bias0_loaded = sem("bias0_loaded")
        least_ready = sem("least_ready")
        log_ready = sem("log_ready")
        bias_ready = sem("bias_ready")
        bias_stored = [sem("bias_stored0"), sem("bias_stored1")]
        cnt_turned = sem("cnt_turned")
        cnt_t_ready = sem("cnt_t_ready")
        cnt_t_used = sem("cnt_t_used")
        conv_ready = sem("conv_ready")
        x1_ready = sem("x1_ready")
        x1_stored = sem("x1_stored")
        agg_steps = sem("agg_steps")

        with nc.Block() as block:
            @block.sync
            def _(sp):
                sp.dma_start(bias0_sb[:, :], bias0.broadcast_to([P, D])).then_inc(bias0_loaded, 16)
                with sp.Fori(0, NT // 2) as i:
                    for b in range(2):
                        t = 2 * i + b
                        sp.wait_ge(conv_ready, t + 1)
                        sp.wait_ge(bias_ready, t + 1)
                        sp.dma_start(cnt[b][:, :], counts_rows[bass.ts(t, P), :]).then_inc(cnt_loaded[b], 16)

            @block.gpsimd
            def _(pool):
                for b in range(2):
                    pool.dma_start(scrap_row, norm[0:1, :]).then_inc(bias_stored[b], 16)
                    pool.wait_ge(bias_stored[b], 16)
                with pool.Fori(0, NT // 2) as i:
                    for b in range(2):
                        t = 2 * i + b
                        pool.wait_ge(bias_ready, t + 3)
                        pool.dma_start(bias_rows[bass.ts(t, P), :], bias[b][:, :]).then_inc(bias_stored[b], 16)
                        pool.wait_ge(x1_ready, t + 2)
                        pool.dma_start(x1_rows[bass.ts(t, P), :], x_sb[:, bass.ds(t, 1), :].rearrange("p o d -> p (o d)")
                                       ).then_inc(x1_stored, 16)
                for b in range(2):
                    pool.wait_ge(bias_stored[b], 16 + 16 * NT // 2)
                pool.wait_ge(x1_stored, 16 * NT)

            @block.tensor
            def _(pe):
                def turn(b, r, k):
                    for j in range(BPC):
                        mm = pe.transpose(turn_ps[r][:, j * P:(j + 1) * P],
                                          cnt[b][:, (k * BPC + j) * P:(k * BPC + j + 1) * P], identity[0:P, 0:P])
                    mm.then_inc(cnt_turned, 1)

                pe.sem_inc(cnt_t_used, 2)
                with pe.Fori(0, NT // 2) as i:
                    for b in range(2):
                        t = 2 * i + b
                        pe.wait_ge(cnt_loaded[b], 16 * (i + 1))
                        pe.wait_ge(x1_ready, t + 1)
                        for k in range(NKC + 1):
                            u = b * NKC + k
                            if k < NKC:
                                pe.wait_ge(cnt_t_ready, 2 * NKC * i + u + 1)
                                turn(b, u % 2, k)
                            if k > 0:
                                pe.wait_ge(cnt_t_ready, 2 * NKC * i + u + 2)
                                for j in range(BPC):
                                    s = (k - 1) * BPC + j
                                    mm = pe.matmul(agg_ps[b][:, :], lhsT=cnt_t[(u - 1) % 2][:, j * P:(j + 1) * P],
                                                   rhs=hw[:, s, :], start=(s == 0), stop=(s == NT - 1))
                                mm.then_inc(cnt_t_used, 1)

            @block.scalar
            def _(act):
                act.sem_inc(cnt_t_ready, 2)
                act.sem_inc(log_ready, 1)
                with act.Fori(0, NT // 2) as i:
                    for b in range(2):
                        t = 2 * i + b
                        for k in range(NKC):
                            u = b * NKC + k
                            act.wait_ge(cnt_turned, 2 * NKC * i + u + 1)
                            act.wait_ge(cnt_t_used, 2 * NKC * i + u + 1)
                            act.copy(cnt_t[u % 2][:, :], turn_ps[u % 2][:, 0:KC]).then_inc(cnt_t_ready, 1)
                        act.wait_ge(least_ready, t + 1)
                        act.activation(logc[:, :], least1[:, :], ACT.Ln).then_inc(log_ready, 1)

            @block.vector
            def _(dve):
                dve.sem_inc(bias_ready, 2)
                dve.sem_inc(conv_ready, 2)
                dve.sem_inc(x1_ready, 1)
                dve.wait_ge(bias0_loaded, 16)
                with dve.Fori(0, NT // 2) as i:
                    steps = Steps(dve, agg_steps, 6 * i)
                    for b in range(2):
                        t = 2 * i + b
                        dve.wait_ge(cnt_loaded[b], 16 * (i + 1))
                        dve.wait_ge(log_ready, t + 1)
                        dve.tensor_scalar(least1[:, :], cnt[b][:, :], 1.0, None, ALU.max).then_inc(least_ready, 1)
                        dve.wait_ge(bias_stored[b], 16 + 16 * i)
                        steps.done(dve.tensor_scalar(bias[b][:, :], cnt[b][:, :], 0.5, MASKED, ALU.is_lt, ALU.mult))
                        steps.wait()
                        dve.wait_ge(log_ready, t + 2)
                        dve.tensor_tensor(bias[b][:, :], bias[b][:, :], logc[:, :], ALU.add).then_inc(bias_ready, 1)
                        dve.wait_ge(cnt_t_used, NKC * (t + 1) + 2)
                        steps.done(dve.scalar_tensor_tensor(conv[:, :], agg_ps[b][:, :], norm[:, bass.ds(t, 1)], bias0_sb[:, :],
                                                            ALU.mult, ALU.add))
                        dve.sem_inc(conv_ready, 1)
                        steps.wait()
                        here = x_sb[:, bass.ds(t, 1), :].rearrange("p o d -> p (o d)")
                        steps.done(dve.scalar_tensor_tensor(here, conv[:, :], 0.0, here, ALU.max, ALU.add))
                        steps.wait()
                        dve.sem_inc(x1_ready, 1)


def second_norm(nc, sem, psum, sb, g):
    xt, x1_rows, identity, eps_col = g["xt"], g["x1_rows"], g["identity"], g["eps_col"]
    with ExitStack() as ctx:
        x1 = sb(ctx, "x1_all", [P, NT, D])
        stats = sb(ctx, "x1_stats", [P, NT, 6])
        mv = sb(ctx, "x1_mv", [P, NT, 2])
        root = sb(ctx, "x1_root", [P, NT])
        rstd = sb(ctx, "x1_rstd", [P, NT])
        shift = sb(ctx, "x1_shift", [P, NT])
        h = [sb(ctx, f"x1_h{b}", [P, D]) for b in range(2)]
        turn_ps = [psum(ctx, f"x1_turn{b}", [128, BANK]) for b in range(2)]
        x1_loaded = sem("x1_loaded")
        n2_steps = sem("n2_steps")
        n2_var = sem("n2_var")
        n2_root = sem("n2_root")
        n2_scales = sem("n2_scales")
        n2_h = sem("n2_h")
        n2_turned = sem("n2_turned")
        n2_copied = sem("n2_copied")
        with nc.Block() as block:
            @block.sync
            def _(sp):
                sp.dma_start(x1[:, :, :], x1_rows.rearrange("(t p) d -> p t d", p=P)).then_inc(x1_loaded, 16)

            @block.vector
            def _(dve):
                steps = Steps(dve, n2_steps)
                dve.sem_inc(n2_copied, 1)
                dve.wait_ge(x1_loaded, 16)
                for t in range(NT):
                    steps.done(dve.bn_stats(stats[:, t, :], x1[:, t, :]))
                steps.wait()
                for t in range(NT):
                    ins = dve.bn_aggr(mv[:, t, :], stats[:, t, :])
                ins.then_inc(n2_var, 1)
                dve.wait_ge(n2_root, 1)
                steps.done(dve.reciprocal(rstd[:, :], root[:, :]))
                steps.wait()
                dve.scalar_tensor_tensor(shift[:, :], mv[:, :, 0], -1.0, rstd[:, :], ALU.mult, ALU.mult).then_inc(n2_scales, 1)
                with dve.Fori(0, NT // 2) as i:
                    for b in range(2):
                        t = 2 * i + b
                        dve.wait_ge(n2_turned, t + 2)
                        dve.tensor_copy(xt[:, :, bass.ts(t, P)],
                                        turn_ps[b][:, 0:FC * P].rearrange("p (c n) -> p c n", c=FC)).then_inc(n2_copied, 1)

            @block.scalar
            def _(act):
                act.wait_ge(n2_var, 1)
                act.activation(root[:, :], mv[:, :, 1], ACT.Sqrt, bias=eps_col[0:P, :]).then_inc(n2_root, 1)
                act.wait_ge(n2_scales, 1)
                with act.Fori(0, NT // 2) as i:
                    for b in range(2):
                        t = 2 * i + b
                        act.wait_ge(n2_turned, t + 1)
                        act.activation(h[b][:, :], x1[:, bass.ds(t, 1), :].rearrange("p o d -> p (o d)"), ACT.Relu,
                                       bias=shift[:, bass.ds(t, 1)], scale=rstd[:, bass.ds(t, 1)]).then_inc(n2_h, 1)

            @block.tensor
            def _(pe):
                pe.sem_inc(n2_turned, 1)
                with pe.Fori(0, NT // 2) as i:
                    for b in range(2):
                        t = 2 * i + b
                        pe.wait_ge(n2_h, t + 1)
                        pe.wait_ge(n2_copied, t + 1)
                        for c in range(FC):
                            mm = pe.transpose(turn_ps[b][:, c * P:(c + 1) * P], h[b][:, c * 128:(c + 1) * 128], identity[0:P, 0:P])
                        mm.then_inc(n2_turned, 1)


def transformer(nc, sem, psum, sb, g):
    with ExitStack() as ctx:
        keys = sb(ctx, "keys", [128, H, N], F16)
        values = sb(ctx, "values", [P, NT, H, 2 * DH], F16)
        vec = sb(ctx, "vec", [128, 30])
        g = dict(g, keys=keys, values=values, vec=vec)
        sems = {}

        def named(name):
            if name not in sems:
                sems[name] = sem(name)
            return sems[name]

        maxed, biased, bank_read = named("maxed"), named("biased"), named("bank_read")
        weighted, agg_out = named("weighted"), named("agg_out")
        products, splits = named("qkv_products"), named("qkv_splits")
        staged = [named("qk_stored0"), named("qk_stored1")]
        with nc.Block() as block:
            @block.sync
            def _(sp):
                for b in range(2):
                    sp.dma_start(g["scrap_row"][:, 0:1], g["eps_col"][0:1, :]).then_inc(staged[b], 16)
                    sp.wait_ge(staged[b], 16)

            @block.vector
            def _(dve):
                dve.sem_inc(products, 1)
                dve.sem_inc(splits, 1)
                dve.sem_inc(maxed, H + 1)
                dve.sem_inc(biased, SB)
                dve.sem_inc(bank_read, TB)
                dve.sem_inc(weighted, TB)
                dve.sem_inc(agg_out, 2)

        with nc.Fori(0, L) as layer:
            projections(nc, named, psum, sb, g, layer)
            attention(nc, named, psum, sb, g, layer)
            feed_forward(nc, named, psum, sb, g, layer)


def projections(nc, sem, psum, sb, g, layer):
    xt, keys, values, vec, q_feat = g["xt"], g["keys"], g["values"], g["vec"], g["q_feat"]
    VB = 2
    with ExitStack() as ctx:
        wq_sb = sb(ctx, "wq_sb", [128, FC, D])
        wk_sb = sb(ctx, "wk_sb", [128, FC, D])
        wv_sb = sb(ctx, "wv_sb", [128, FC, D])
        bq8 = sb(ctx, "bq8", [128, FC])
        xc = [sb(ctx, f"xc{b}", [128, FC, CH]) for b in range(2)]
        qf = sb(ctx, "qf", [128, FC, CH])
        q_hi = [sb(ctx, f"q_hi{b}", [128, FC, CH], F16) for b in range(2)]
        q_lo = [sb(ctx, f"q_lo{b}", [128, FC, CH], F16) for b in range(2)]
        k_hi = [sb(ctx, f"k_hi{b}", [128, FC, CH], F16) for b in range(2)]
        k_lo = [sb(ctx, f"k_lo{b}", [128, FC, CH], F16) for b in range(2)]
        q_ps = psum(ctx, "q_ps", [128, 2, BANK])
        k_ps = psum(ctx, "k_ps", [128, 2, BANK])
        v_ps = psum(ctx, "v_ps", [P, VB, BANK])

        qkv_loaded = sem("qkv_loaded")
        bq_ready = sem("bq_ready")
        xc_ready = sem("xc_ready")
        products = sem("qkv_products")
        q_scaled = sem("q_scaled")
        halves = sem("high_halves")
        splits = sem("qkv_splits")
        staged = [sem("qk_stored0"), sem("qk_stored1")]
        STORED = 6 * 16

        def bank_view(ps):
            return ps[:, :, 0:2 * CH]

        def pairs(tile):
            return tile[:, :, :].rearrange("p (a c) n -> p a (c n)", a=2)

        with nc.Block() as block:
            @block.sync
            def _(sp):
                rows = bass.ts(layer, 128)
                for tile, w in ((wq_sb, g["wq"]), (wk_sb, g["wk"]), (wv_sb, g["wv"])):
                    sp.dma_start(tile[:, :, :].rearrange("p c d -> p (c d)"), w[rows, :]).then_inc(qkv_loaded, 16)
                sp.dma_start(vec[:, :], g["vectors"][rows, :]).then_inc(qkv_loaded, 16)
                with sp.Fori(0, NCH // 2) as i:
                    for b in range(2):
                        c = 2 * i + b
                        nodes = bass.ts(c, CH)
                        sp.wait_ge(splits, 3 * NCH * layer + 3 * c + 2)
                        apart(sp, g["waits_met"])
                        for part, tile in ((0, q_hi[b]), (1, q_lo[b])):
                            sp.dma_start(q_feat[part * D:(part + 1) * D, nodes].rearrange("(c p) n -> p c n", p=128),
                                         tile[:, :, :]).then_inc(staged[b], 16)
                        sp.wait_ge(splits, 3 * NCH * layer + 3 * c + 3)
                        apart(sp, g["waits_met"])
                        for part, tile in ((0, k_hi[b]), (1, k_lo[b])):
                            for odd in range(2):
                                sp.dma_start(keys[64 * part:64 * part + 64, odd::2, nodes],
                                             tile[64 * odd:64 * odd + 64, :, :]).then_inc(staged[b], 16)
                for b in range(2):
                    sp.wait_ge(staged[b], STORED * (NCH // 2) * (layer + 1) + 16)
                    apart(sp, g["waits_met"])

            @block.gpsimd
            def _(pool):
                with pool.Fori(0, NCH // 2) as i:
                    for b in range(2):
                        c = 2 * i + b
                        pool.wait_ge(products, 3 * NCH * layer + 3 * c + 1)
                        pool.tensor_copy(xc[b][:, :, :], xt[:, :, bass.ts(c, CH)]).then_inc(xc_ready, 1)

            @block.tensor
            def _(pe):
                pe.wait_ge(qkv_loaded, 64 * (layer + 1))
                apart(pe, g["waits_met"])
                with pe.Fori(0, NCH // 2) as i:
                    for b in range(2):
                        c = 2 * i + b
                        pe.wait_ge(xc_ready, NCH * layer + c + 1)
                        pe.wait_ge(splits, 3 * NCH * layer + 3 * c + 1)
                        for w, ps in ((wq_sb, q_ps), (wk_sb, k_ps)):
                            for o in range(FC):
                                for k in range(FC):
                                    mm = pe.matmul(ps[:, o // 2, (o % 2) * CH:(o % 2 + 1) * CH],
                                                   lhsT=w[:, k, o * 128:(o + 1) * 128], rhs=xc[b][:, k, :],
                                                   start=(k == 0), stop=(k == FC - 1))
                            mm.then_inc(products, 1)
                        for v in range(VB):
                            for k in range(FC):
                                mm = pe.matmul(v_ps[:, v, :], lhsT=xc[b][:, k, v * P:(v + 1) * P], rhs=wv_sb[:, k, :],
                                               start=(k == 0), stop=(k == FC - 1))
                        mm.then_inc(products, 1)

            @block.scalar
            def _(act):
                act.wait_ge(qkv_loaded, 64 * (layer + 1))
                act.activation(bq8[:, :], vec[:, 0:FC], ACT.Copy, scale=SCALING).then_inc(bq_ready, 1)
                act.wait_ge(bq_ready, layer + 1)
                with act.Fori(0, NCH // 2) as i:
                    for b in range(2):
                        c = 2 * i + b
                        base = 3 * NCH * layer + 3 * c
                        act.wait_ge(products, base + 2)
                        act.wait_ge(splits, base + 1)
                        for o in range(FC):
                            act.activation(qf[:, o, :], q_ps[:, o // 2, (o % 2) * CH:(o % 2 + 1) * CH], ACT.Identity,
                                           bias=bq8[:, o:o + 1], scale=SCALING).then_inc(q_scaled, 1)
                        act.wait_ge(staged[b], STORED * ((NCH // 2) * layer + i) + 16)
                        act.wait_ge(q_scaled, FC * (NCH * layer + c + 1))
                        act.copy(q_hi[b][:, :, :], qf[:, :, :]).then_inc(halves, 1)
                        act.wait_ge(products, base + 3)
                        act.copy(pairs(k_hi[b]), bank_view(k_ps)).then_inc(halves, 1)
                        act.wait_ge(products, base + 4)
                        act.copy(values[:, bass.ts(c, VB), :, 0:DH],
                                 v_ps[:, :, :].rearrange("p v (h d) -> p v h d", h=H)).then_inc(halves, 1)

            @block.vector
            def _(dve):
                with dve.Fori(0, NCH // 2) as i:
                    for b in range(2):
                        c = 2 * i + b
                        base = 3 * NCH * layer + 3 * c
                        dve.wait_ge(halves, base + 1)
                        dve.tensor_tensor(q_lo[b][:, :, :], qf[:, :, :], q_hi[b][:, :, :], ALU.subtract).then_inc(splits, 1)
                        dve.wait_ge(halves, base + 2)
                        dve.tensor_tensor(pairs(k_lo[b]), bank_view(k_ps), pairs(k_hi[b]), ALU.subtract).then_inc(splits, 1)
                        dve.wait_ge(halves, base + 3)
                        for v in range(VB):
                            here = values[:, bass.ds(VB * c + v, 1), :, :].rearrange("p o h d -> p (o h) d")
                            ins = dve.tensor_tensor(here[:, :, DH:2 * DH], v_ps[:, v, :].rearrange("p (h d) -> p h d", h=H),
                                                    here[:, :, 0:DH], ALU.subtract)
                        ins.then_inc(splits, 1)


def attention(nc, sem, psum, sb, g, layer):
    xt, keys, values, vec, q_feat = g["xt"], g["keys"], g["values"], g["vec"], g["q_feat"]
    bias_rows, identity = g["bias_rows"], g["identity"]
    HEADS = NT * H
    TURN_SUMS, TIMES_WO = -1, -2
    EXPS = ((0, 2), (2, 4), (4, 5))
    with ExitStack() as ctx:
        wo_sb = sb(ctx, "wo_sb", [128, FC, D])
        queries = [sb(ctx, f"queries{b}", [128, H, 2, P], F16) for b in range(2)]
        bias = [sb(ctx, f"mask{b}", [P, N]) for b in range(2)]
        prob = [sb(ctx, f"prob{r}", [P, N]) for r in range(4)]
        chunk_max = [sb(ctx, f"chunk_max{r}", [P, NKC]) for r in range(4)]
        scrap = sb(ctx, "scrap", [P, NKC])
        neg_max = [sb(ctx, f"neg_max{r}", [P, 1]) for r in range(4)]
        sums = [sb(ctx, f"sums{b}", [P, H, len(EXPS)]) for b in range(2)]
        total = sb(ctx, "total", [P, H])
        total_eps = sb(ctx, "total_eps", [P, H])
        inverse = sb(ctx, "inverse", [P, H])
        p_hi = [sb(ctx, f"p_hi{r}", [P, KC], F16) for r in range(TB)]
        p_lo = [sb(ctx, f"p_lo{r}", [P, KC], F16) for r in range(TB)]
        by_high = [sb(ctx, f"by_high{r}", [P, DH]) for r in range(2)]
        agg_sb = [sb(ctx, f"agg{b}", [128, H * DH]) for b in range(2)]
        agg = [a[0:P, :].rearrange("p (h d) -> p h d", h=H) for a in agg_sb]
        agg_t = [a[:, 0:FC * P] for a in agg_sb]
        s_ps = [psum(ctx, f"s_ps{r}", [P, BANK]) for r in range(SB)]
        t_ps = [psum(ctx, f"t_ps{r}", [128, BANK]) for r in range(TB)]
        o_ps = [psum(ctx, f"o_ps{r}", [P, BANK]) for r in range(2)]

        wo_loaded = sem("wo_loaded")
        q_loaded = [sem("q_loaded0"), sem("q_loaded1")]
        mask_loaded = [sem("mask_loaded0"), sem("mask_loaded1")]
        scored = sem("scored")
        biased = sem("biased")
        maxed = sem("maxed")
        exped = sem("exped")
        turned = sem("turned")
        bank_read = sem("bank_read")
        p_high = sem("p_high")
        weighted = sem("weighted")
        high_out = sem("high_out")
        agg_out = sem("agg_out")
        agg_ready = sem("agg_ready")
        steps_att = sem("steps_att")

        def loads(sp):
            with sp.Fori(0, NT // 2) as i:
                for b in range(2):
                    t = 2 * i + b
                    sp.wait_ge(maxed, HEADS * layer + H * t + 1)
                    for part in range(2):
                        for half in range(2):
                            sp.dma_start(queries[b][64 * half:64 * half + 64, :, part, :],
                                         q_feat[part * D:(part + 1) * D, bass.ts(t, P)].rearrange("(h d) n -> d h n", h=H)
                                         ).then_inc(q_loaded[b], 16)
                    sp.dma_start(bias[b][:, :], bias_rows[bass.ts(t, P), :]).then_inc(mask_loaded[b], 16)

        def unit(j):
            return j % H, (j // H) % 2

        def use(i, j, k):
            t, h = j // H, j % H
            if isinstance(i, int) and i == 0 and j < HEAD0:
                n = NKC * h + k
            elif k == TURN_SUMS:
                n = USES * t - 2 + 2 * NKC
            elif k == TIMES_WO:
                n = USES * t - 2 + 3 * NKC + 1
            else:
                n = USES * t - 2 + NKC * h + k + (h >= 2) + (h >= 3)
            return USES * NT * layer + 2 * USES * i + n, n % TB

        def last_use(k):
            n = USES * NT - 2 + k
            return USES * NT * layer + n, n % TB

        with nc.Block() as block:
            @block.sync
            def _(sp):
                sp.dma_start(wo_sb[:, :, :].rearrange("p c d -> p (c d)"), g["wo"][bass.ts(layer, 128), :]).then_inc(wo_loaded, 16)
                loads(sp)

            @block.tensor
            def _(pe):
                def score(i, j, c):
                    h, b = unit(j)
                    m = HEADS * layer + UNITS * i + j
                    if h == 0 and c == 0:
                        pe.wait_ge(q_loaded[b], 64 * ((NT // 2) * layer + i + j // UNITS + 1))
                    pe.wait_ge(biased, NKC * m + c + 1)
                    for part in range(2):
                        mm = pe.matmul(s_ps[(NKC * j + c) % SB][:, 0:KC], lhsT=queries[b][:, h, part, :],
                                       rhs=keys[:, h, c * KC:(c + 1) * KC], start=(part == 0), stop=(part == 1))
                    mm.then_inc(scored, 1)

                def turn_weights(i, j, k):
                    n, r = use(i, j, k)
                    if k == 0:
                        pe.wait_ge(exped, len(EXPS) * (HEADS * layer + UNITS * i + j + 1))
                    pe.wait_ge(bank_read, n + 1)
                    for s in range(BPC):
                        mm = pe.transpose(t_ps[r][0:P, s * P:(s + 1) * P],
                                          prob[j % 4][:, (k * BPC + s) * P:(k * BPC + s + 1) * P], identity[0:P, 0:P])
                    mm.then_inc(turned, 1)

                def weigh(i, j, k):
                    n, r = use(i, j, k)
                    if k == 0:
                        pe.wait_ge(agg_out, HEADS * layer + UNITS * i + j + 1)
                    pe.wait_ge(bank_read, n + TB + 1)
                    p = (NKC * j + k) % TB
                    for s in range(BPC):
                        for half, weights in enumerate((p_hi[p], p_lo[p])):
                            mm = pe.matmul(o_ps[j % 2][:, 0:2 * DH], lhsT=weights[:, s * P:(s + 1) * P],
                                           rhs=values[:, k * BPC + s, j % H, :],
                                           start=(k == 0 and s == 0 and half == 0),
                                           stop=(k == NKC - 1 and s == BPC - 1 and half == 1))
                    mm.then_inc(weighted, 1)

                def turn_sums(tile, b, n, r):
                    pe.wait_ge(agg_ready, tile + 1)
                    pe.wait_ge(bank_read, n + 1)
                    flat = agg_sb[b][0:P, :]
                    for c in range(FC):
                        mm = pe.transpose(t_ps[r][:, c * P:(c + 1) * P], flat[:, c * 128:(c + 1) * 128], identity[0:P, 0:P])
                    mm.then_inc(turned, 1)

                def times_wo(b, n, r, turned_use):
                    pe.wait_ge(bank_read, turned_use + TB + 1)
                    pe.wait_ge(bank_read, n + 1)
                    for o in range(FC):
                        for k in range(FC):
                            mm = pe.matmul(t_ps[r][:, o * P:(o + 1) * P], lhsT=wo_sb[:, k, o * 128:(o + 1) * 128],
                                           rhs=agg_t[b][:, k * P:(k + 1) * P], start=(k == 0), stop=(k == FC - 1))
                    mm.then_inc(turned, 1)

                def units(i, j0, j1, last):
                    for j in range(j0, j1):
                        for k in range(NKC):
                            turn_weights(i, j, k)
                            if not (last and j + 2 >= UNITS):
                                score(i, j + 2, k)
                            if k >= 2:
                                weigh(i, j, k - 2)
                            elif j > 0:
                                weigh(i, j - 1, NKC - 2 + k)
                        if j % H == 1 and j > H:
                            turn_sums(NT * layer + 2 * i + j // H - 1, (j // H - 1) % 2, *use(i, j, TURN_SUMS))
                        if j % H == 2 and j > H:
                            times_wo((j // H - 1) % 2, *use(i, j, TIMES_WO), use(i, j, TURN_SUMS)[0])

                pe.wait_ge(wo_loaded, 16 * (layer + 1))
                for j in range(2):
                    for c in range(NKC):
                        score(0, j, c)
                units(0, 0, HEAD0, False)
                with pe.Fori(0, NT // 2 - 1) as i:
                    units(i, HEAD0, HEAD0 + UNITS, False)
                units(NT // 2 - 1, HEAD0, UNITS, True)
                for k in range(2):
                    weigh(NT // 2 - 1, UNITS - 1, NKC - 2 + k)
                turn_sums(NT * layer + NT - 1, 1, *last_use(0))
                times_wo(1, *last_use(1), last_use(0)[0])

            @block.scalar
            def _(act):
                def exps(i, j, piece):
                    h, b = unit(j)
                    if piece == 0:
                        act.wait_ge(maxed, HEADS * layer + UNITS * i + j + 1 + H + 1)
                    c0, c1 = EXPS[piece]
                    here = prob[j % 4][:, c0 * KC:c1 * KC]
                    act.activation(here, here, ACT.Exp, bias=neg_max[j % 4][:, :],
                                   accum_out=sums[b][:, h, piece:piece + 1]).then_inc(exped, 1)

                def high_half(i, j, k):
                    n, r = use(i, j, k)
                    act.wait_ge(turned, n + 1)
                    act.wait_ge(weighted, NKC * (HEADS * layer + UNITS * i + j) + k + 1)
                    act.copy(p_hi[(NKC * j + k) % TB][:, :], t_ps[r][0:P, 0:KC]).then_inc(p_high, 1)

                def read_high(i, j):
                    n = HEADS * layer + UNITS * i + j
                    act.wait_ge(weighted, NKC * (n + 1) + TB)
                    act.wait_ge(agg_out, n + 1)
                    act.copy(by_high[j % 2][:, :], o_ps[j % 2][:, 0:DH]).then_inc(high_out, 1)

                def turned_sums(b, n, r):
                    act.wait_ge(turned, n + 1)
                    act.copy(agg_t[b], t_ps[r][:, 0:FC * P]).then_inc(bank_read, 1)

                def units(i, j0, j1, last):
                    for j in range(j0, j1):
                        for k in range(NKC):
                            high_half(i, j, k)
                            if k == 2 and j > 0:
                                read_high(i, j - 1)
                            if k % 2 == 0 and not (last and j + 1 >= UNITS):
                                exps(i, j + 1, k // 2)
                        if j % H == 1 and j > H:
                            turned_sums((j // H - 1) % 2, *use(i, j, TURN_SUMS))

                for piece in range(len(EXPS)):
                    exps(0, 0, piece)
                units(0, 0, HEAD0, False)
                with act.Fori(0, NT // 2 - 1) as i:
                    units(i, HEAD0, HEAD0 + UNITS, False)
                units(NT // 2 - 1, HEAD0, UNITS, True)
                read_high(NT // 2 - 1, UNITS - 1)
                turned_sums(1, *last_use(0))

            @block.vector
            def _(dve):
                def add_bias(i, j, c):
                    h, b = unit(j)
                    m = HEADS * layer + UNITS * i + j
                    if h == 0 and c == 0:
                        dve.wait_ge(mask_loaded[b], 16 * ((NT // 2) * layer + i + j // UNITS + 1))
                    dve.wait_ge(scored, NKC * m + c + 1)
                    apart(dve, g["waits_met"])
                    at = slice(c * KC, (c + 1) * KC)
                    dve.tensor_tensor_reduce(out=prob[j % 4][:, at], in0=s_ps[(NKC * j + c) % SB][:, 0:KC], in1=bias[b][:, at],
                                             scale=1.0, scalar=MASKED, op0=ALU.add, op1=ALU.max,
                                             accum_out=chunk_max[j % 4][:, c:c + 1]).then_inc(biased, 1)

                def maximum(i, j):
                    m = HEADS * layer + UNITS * i + j
                    dve.wait_ge(biased, NKC * (m + 1) + SB)
                    dve.tensor_scalar(scrap[:, :], chunk_max[j % 4][:, :], -1.0, -FLOOR, ALU.mult, ALU.min,
                                      accum_out=neg_max[j % 4][:, :]).then_inc(maxed, 1)

                def low_half(i, j, k):
                    n, r = use(i, j, k)
                    p = (NKC * j + k) % TB
                    dve.wait_ge(p_high, NKC * (HEADS * layer + UNITS * i + j) + k + 1)
                    dve.tensor_tensor(p_lo[p][:, :], t_ps[r][0:P, 0:KC], p_hi[p][:, :],
                                      ALU.subtract).then_inc(bank_read, 1)

                def read_low(i, j):
                    n = HEADS * layer + UNITS * i + j
                    dve.wait_ge(high_out, n + 1)
                    dve.tensor_tensor(agg[(j // H) % 2][:, j % H, :], o_ps[j % 2][:, DH:2 * DH], by_high[j % 2][:, :],
                                      ALU.add).then_inc(agg_out, 1)

                def normalise(i, j):
                    b = (j // H) % 2
                    steps = Steps(dve, steps_att, 3 * (NT * layer + 2 * i + j // H))
                    steps.done(dve.tensor_reduce(total[:, :], sums[b][:, :, :], AXX, ALU.add))
                    steps.wait()
                    steps.done(dve.tensor_scalar(total_eps[:, :], total[:, :], 1e-16, None, ALU.add))
                    steps.wait()
                    steps.done(dve.reciprocal(inverse[:, :], total_eps[:, :]))
                    steps.wait()
                    dve.wait_ge(agg_out, HEADS * layer + UNITS * i + j + 1 + 2)
                    dve.tensor_tensor(agg[b][:, :, :], agg[b][:, :, :], inverse[:, :].unsqueeze(2).broadcast_to([P, H, DH]),
                                      ALU.mult).then_inc(agg_ready, 1)

                def add_output(tile, n, r):
                    dve.wait_ge(turned, n + 1)
                    nodes = bass.ts(tile, P)
                    for o in range(FC):
                        ins = dve.scalar_tensor_tensor(xt[:, o, nodes], t_ps[r][:, o * P:(o + 1) * P],
                                                       vec[:, FC + o:FC + o + 1], xt[:, o, nodes], ALU.add, ALU.add)
                    ins.then_inc(bank_read, 1)

                def units(i, j0, j1, last):
                    for j in range(j0, j1):
                        for k in range(NKC):
                            low_half(i, j, k)
                            if k == 3 and j > 0:
                                read_low(i, j - 1)
                            if not (last and j + 2 >= UNITS):
                                add_bias(i, j + 2, k)
                        if not (last and j + 2 >= UNITS):
                            maximum(i, j + 2)
                        if j % H == 0 and j > 0:
                            normalise(i, j - 1)
                        if j % H == 2 and j > H:
                            add_output(2 * i + j // H - 1, *use(i, j, TIMES_WO))

                for j in range(2):
                    for c in range(NKC):
                        add_bias(0, j, c)
                    maximum(0, j)
                units(0, 0, HEAD0, False)
                with dve.Fori(0, NT // 2 - 1) as i:
                    units(i, HEAD0, HEAD0 + UNITS, False)
                units(NT // 2 - 1, HEAD0, UNITS, True)
                read_low(NT // 2 - 1, UNITS - 1)
                normalise(NT // 2 - 1, UNITS - 1)
                add_output(NT - 1, *last_use(1))


def feed_forward(nc, sem, psum, sb, g, layer):
    xt, vec, eps_col = g["xt"], g["vec"], g["eps_col"]
    SC = 500
    with ExitStack() as ctx:
        w1_sb = sb(ctx, "w1_sb", [128, FC, FF])
        w2_sb = sb(ctx, "w2_sb", [128, HC, D])
        stats = sb(ctx, "bn_stats", [128, FC, N // SC, 6])
        mv = sb(ctx, "bn_mv", [128, FC, 2])
        root = sb(ctx, "bn_root", [128, FC])
        rstd = sb(ctx, "bn_rstd", [128, FC])
        gain = sb(ctx, "bn_gain", [128, FC])
        taken = sb(ctx, "bn_taken", [128, FC])
        shift = sb(ctx, "bn_shift", [128, FC])
        x2 = [sb(ctx, f"x2_{b}", [128, FC, CH]) for b in range(2)]
        hid = [sb(ctx, f"hid{b}", [128, HC, CH]) for b in range(2)]
        hid_ps = [psum(ctx, f"hid_ps{b}", [128, BANK]) for b in range(2)]
        y_ps = [psum(ctx, f"y_ps{b}", [128, 2, BANK]) for b in range(2)]

        w12_loaded = sem("w12_loaded")
        ff_steps = sem("ff_steps")
        ff_var = sem("ff_var")
        ff_root = sem("ff_root")
        x2_ready = sem("x2_ready")
        hid_summed = sem("hid_summed")
        hid_ready = sem("hid_ready")
        y_summed = sem("y_summed")
        y_added = sem("y_added")
        NORM = FC * (N // SC) + FC + 4

        with nc.Block() as block:
            @block.sync
            def _(sp):
                rows = bass.ts(layer, 128)
                sp.dma_start(w1_sb[:, :, :].rearrange("p c d -> p (c d)"), g["w1"][rows, :]).then_inc(w12_loaded, 16)
                sp.dma_start(w2_sb[:, :, :].rearrange("p c d -> p (c d)"), g["w2"][rows, :]).then_inc(w12_loaded, 16)

            @block.vector
            def _(dve):
                steps = Steps(dve, ff_steps, 2 * NORM * layer)

                def statistics(number, gamma, beta):
                    for o in range(FC):
                        for c in range(N // SC):
                            steps.done(dve.bn_stats(stats[:, o, c, :], xt[:, o, c * SC:(c + 1) * SC]))
                    steps.wait()
                    apart(dve, g["waits_met"])
                    for o in range(FC):
                        steps.done(dve.bn_aggr(mv[:, o, :], stats[:, o, :, :].rearrange("p c s -> p (c s)")))
                    steps.wait()
                    dve.sem_inc(ff_var, 1)
                    dve.wait_ge(ff_root, 2 * layer + number + 1)
                    steps.done(dve.reciprocal(rstd[:, :], root[:, :]))
                    steps.wait()
                    steps.done(dve.tensor_tensor(gain[:, :], rstd[:, :], vec[:, gamma:gamma + FC], ALU.mult))
                    steps.wait()
                    steps.done(dve.tensor_tensor(taken[:, :], mv[:, :, 0], gain[:, :], ALU.mult))
                    steps.wait()
                    steps.done(dve.tensor_tensor(shift[:, :], vec[:, beta:beta + FC], taken[:, :], ALU.subtract))
                    steps.wait()
                    apart(dve, g["waits_met"])

                statistics(0, 2 * FC, 3 * FC)
                with dve.Fori(0, NCH // 2) as i:
                    for b in range(2):
                        c = 2 * i + b
                        nodes = bass.ts(c, CH)
                        for o in range(FC):
                            dve.tensor_scalar(x2[b][:, o, :], xt[:, o, nodes], gain[:, o:o + 1], shift[:, o:o + 1],
                                              ALU.mult, ALU.add).then_inc(x2_ready, 1)
                        dve.wait_ge(x2_ready, FC * (NCH * layer + c + 1))
                        dve.wait_ge(y_summed, NCH * layer + c + 1)
                        for o in range(FC):
                            dve.scalar_tensor_tensor(xt[:, o, nodes], y_ps[b][:, o // 2, (o % 2) * CH:(o % 2 + 1) * CH],
                                                     vec[:, 6 * FC + o:6 * FC + o + 1], x2[b][:, o, :], ALU.add, ALU.add
                                                     ).then_inc(y_added, 1)
                dve.wait_ge(y_added, FC * NCH * (layer + 1))
                statistics(1, 4 * FC, 5 * FC)
                for o in range(FC):
                    dve.tensor_scalar(xt[:, o, :], xt[:, o, :], gain[:, o:o + 1], shift[:, o:o + 1], ALU.mult, ALU.add)
                assert steps.n == 2 * NORM

            @block.scalar
            def _(act):
                act.wait_ge(ff_var, 2 * layer + 1)
                act.activation(root[:, :], mv[:, :, 1], ACT.Sqrt, bias=eps_col[:, :]).then_inc(ff_root, 1)
                with act.Fori(0, NCH // 2) as i:
                    for b in range(2):
                        c = 2 * i + b
                        act.wait_ge(hid_summed, NCH * layer + c + 1)
                        for o in range(HC):
                            act.activation(hid[b][:, o, :], hid_ps[b][:, o * CH:(o + 1) * CH], ACT.Relu,
                                           bias=vec[:, 7 * FC + o:7 * FC + o + 1]).then_inc(hid_ready, 1)
                act.wait_ge(ff_var, 2 * layer + 2)
                act.activation(root[:, :], mv[:, :, 1], ACT.Sqrt, bias=eps_col[:, :]).then_inc(ff_root, 1)

            @block.tensor
            def _(pe):
                pe.wait_ge(w12_loaded, 32 * (layer + 1))
                apart(pe, g["waits_met"])
                with pe.Fori(0, NCH // 2) as i:
                    for b in range(2):
                        c = 2 * i + b
                        pe.wait_ge(x2_ready, FC * (NCH * layer + c + 1))
                        for o in range(HC):
                            for k in range(FC):
                                mm = pe.matmul(hid_ps[b][:, o * CH:(o + 1) * CH], lhsT=w1_sb[:, k, o * 128:(o + 1) * 128],
                                               rhs=x2[b][:, k, :], start=(k == 0), stop=(k == FC - 1))
                        mm.then_inc(hid_summed, 1)
                        pe.wait_ge(hid_ready, HC * (NCH * layer + c + 1))
                        for o in range(FC):
                            for k in range(HC):
                                mm = pe.matmul(y_ps[b][:, o // 2, (o % 2) * CH:(o % 2 + 1) * CH],
                                               lhsT=w2_sb[:, k, o * 128:(o + 1) * 128], rhs=hid[b][:, k, :],
                                               start=(k == 0), stop=(k == HC - 1))
                        mm.then_inc(y_summed, 1)


def final_norm(nc, sem, psum, sb, g):
    xt, x1_rows, identity, eps_col, out = g["xt"], g["x1_rows"], g["identity"], g["eps_col"], g["out"]
    with ExitStack() as ctx:
        lng_sb = sb(ctx, "lng_sb", [P, D])
        lnb_sb = sb(ctx, "lnb_sb", [P, D])
        x1 = [sb(ctx, f"x1_{b}", [P, D]) for b in range(2)]
        x1b = [sb(ctx, f"x1b_{b}", [P, D]) for b in range(2)]
        stats = [sb(ctx, f"ln_stats{b}", [P, 6]) for b in range(2)]
        mv = [sb(ctx, f"ln_mv{b}", [P, 2]) for b in range(2)]
        root = [sb(ctx, f"ln_root{b}", [P, 1]) for b in range(2)]
        rstd = [sb(ctx, f"ln_rstd{b}", [P, 1]) for b in range(2)]
        xf = [sb(ctx, f"xf{b}", [128, FC, P]) for b in range(2)]
        unit = sb(ctx, "ln_unit", [P, D])
        scaled = sb(ctx, "ln_scaled", [P, D])
        res = [sb(ctx, f"res{b}", [P, D]) for b in range(2)]
        turn_ps = [psum(ctx, f"ln_turn{b}", [P, BANK]) for b in range(2)]
        ln_loaded = sem("ln_loaded")
        x1_back = [sem("x1_back0"), sem("x1_back1")]
        x1b_ready = sem("x1b_ready")
        xf_ready = sem("xf_ready")
        ln_turned = sem("ln_turned")
        ln_var = sem("ln_var")
        ln_root = sem("ln_root_ready")
        ln_steps = sem("ln_steps")
        res_ready = sem("res_ready")
        res_stored = [sem("res_stored0"), sem("res_stored1")]
        PER = 6
        with nc.Block() as block:
            @block.sync
            def _(sp):
                sp.dma_start(lng_sb[:, :], g["lng"].broadcast_to([P, D])).then_inc(ln_loaded, 16)
                sp.dma_start(lnb_sb[:, :], g["lnb"].broadcast_to([P, D])).then_inc(ln_loaded, 16)
                with sp.Fori(0, NT // 2) as i:
                    for b in range(2):
                        sp.wait_ge(x1b_ready, 2 * i + b + 1)
                        sp.dma_start(x1[b][:, :], x1_rows[bass.ts(2 * i + b, P), :]).then_inc(x1_back[b], 16)

            @block.gpsimd
            def _(pool):
                pool.wait_ge(ln_loaded, 32)
                pool.sem_inc(x1b_ready, 1)
                with pool.Fori(0, NT // 2) as i:
                    for b in range(2):
                        t = 2 * i + b
                        pool.wait_ge(ln_turned, t + 1)
                        pool.tensor_copy(xf[b][:, :, :], xt[:, :, bass.ts(t, P)]).then_inc(xf_ready, 1)
                        pool.wait_ge(x1_back[b], 16 * (i + 1))
                        pool.wait_ge(res_ready, t + 1)
                        pool.tensor_tensor(x1b[b][:, :], x1[b][:, :], lnb_sb[:, :], ALU.add).then_inc(x1b_ready, 1)

            @block.tensor
            def _(pe):
                pe.sem_inc(ln_turned, 1)
                with pe.Fori(0, NT // 2) as i:
                    for b in range(2):
                        t = 2 * i + b
                        pe.wait_ge(xf_ready, t + 1)
                        pe.wait_ge(res_ready, t + 1)
                        for c in range(FC):
                            mm = pe.transpose(turn_ps[b][:, c * 128:(c + 1) * 128], xf[b][:, c, :], identity[:, :])
                        mm.then_inc(ln_turned, 1)

            @block.scalar
            def _(act):
                for b in range(2):
                    act.dma_start(g["scrap_row"][:, 0:1], eps_col[0:1, :]).then_inc(res_stored[b], 16)
                    act.wait_ge(res_stored[b], 16)
                with act.Fori(0, NT // 2) as i:
                    for b in range(2):
                        t = 2 * i + b
                        act.wait_ge(ln_var, t + 1)
                        act.activation(root[b][:, :], mv[b][:, 1:2], ACT.Sqrt, bias=eps_col[0:P, :]).then_inc(ln_root, 1)
                        act.wait_ge(res_ready, t + 2)
                        act.dma_start(out[bass.ts(t, P), :], res[b][:, :]).then_inc(res_stored[b], 16)
                for b in range(2):
                    act.wait_ge(res_stored[b], 16 * (NT // 2) + 16)

            @block.vector
            def _(dve):
                dve.wait_ge(ln_loaded, 32)
                dve.sem_inc(res_ready, 1)
                with dve.Fori(0, NT // 2) as i:
                    steps = Steps(dve, ln_steps, 2 * PER * i)
                    for b in range(2):
                        t = 2 * i + b
                        dve.wait_ge(ln_turned, t + 2)
                        steps.done(dve.bn_stats(stats[b][:, :], turn_ps[b][:, :]))
                        steps.wait()
                        apart(dve, g["waits_met"])
                        steps.done(dve.bn_aggr(mv[b][:, :], stats[b][:, :]))
                        steps.wait()
                        dve.sem_inc(ln_var, 1)
                        dve.wait_ge(ln_root, t + 1)
                        steps.done(dve.reciprocal(rstd[b][:, :], root[b][:, :]))
                        steps.wait()
                        steps.done(dve.tensor_scalar(unit[:, :], turn_ps[b][:, :], mv[b][:, 0:1], rstd[b][:, 0:1],
                                                     ALU.subtract, ALU.mult))
                        steps.wait()
                        steps.done(dve.tensor_tensor(scaled[:, :], unit[:, :], lng_sb[:, :], ALU.mult))
                        steps.wait()
                        dve.wait_ge(x1b_ready, t + 2)
                        dve.wait_ge(res_stored[b], 16 * i + 16)
                        steps.done(dve.tensor_tensor(res[b][:, :], scaled[:, :], x1b[b][:, :], ALU.add))
                        steps.wait()
                        dve.sem_inc(res_ready, 1)
                    assert steps.n == 2 * PER


def kernel(**inputs):
    import numpy as np
    import concourse.bacc as bacc
    from concourse.bass_utils import run_bass_kernel_spmd

    def get(name):
        return np.asarray(inputs[name])

    def turned(w):
        layers, o, k = w.shape
        return np.ascontiguousarray(w.transpose(0, 2, 1).reshape(layers, k // 128, 128, o)
                                    .transpose(0, 2, 1, 3).reshape(layers * 128, (k // 128) * o))

    def columns(v):
        layers, f = v.shape
        return v.reshape(layers, f // 128, 128).transpose(0, 2, 1).reshape(layers * 128, f // 128)

    src, dst = get("src"), get("dst")
    t = "L1_gnn_"
    arrays = {
        "x": np.ascontiguousarray(get("x")),
        "src_cols": np.ascontiguousarray(src.reshape(NCOL, EP).T),
        "dst_cols": np.ascontiguousarray(dst.reshape(NCOL, EP).T),
        "src_row": np.ascontiguousarray(src.reshape(1, E)),
        "dst_row": np.ascontiguousarray(dst.reshape(1, E)),
        "w0": np.ascontiguousarray(get("L0_gnn_weight")),
        "bias0": np.ascontiguousarray(get("L0_gnn_bias").reshape(1, D)),
        "wq": turned(get(t + "Wq")), "wk": turned(get(t + "Wk")), "wv": turned(get(t + "Wv")),
        "wo": turned(get(t + "Wo")), "w1": turned(get(t + "W1")), "w2": turned(get(t + "W2")),
        "vectors": np.ascontiguousarray(np.concatenate(
            [columns(get(t + n)) for n in ("bq", "bo", "g1", "beta1", "g2", "beta2", "b2", "b1")], axis=1)),
        "lng": np.ascontiguousarray(get(t + "ln_g").reshape(1, D)),
        "lnb": np.ascontiguousarray(get(t + "ln_b").reshape(1, D)),
    }
    nc = bacc.Bacc("TRN2", target_bir_lowering=False, num_devices=1)
    args = [nc.dram_tensor(n, a.shape, mybir.dt.from_np(a.dtype), kind="ExternalInput").ap() for n, a in arrays.items()]
    args.append(nc.dram_tensor("out", (N, D), F32, kind="ExternalOutput").ap())
    gnn_kernel(nc, *args)
    r = run_bass_kernel_spmd(nc, [arrays], core_ids=[0])
    return r.results[0]["out"]
```
